# Optimizing a Trainium2 kernel written in Bass

```python
import numpy as np
import jax
import jax.numpy as jnp

def _softmax(x, axis=-1):
    return jax.nn.softmax(x, axis=axis)

def _gelu(x):
    return jax.nn.gelu(x, approximate=True)

def _silu(x):
    return jax.nn.silu(x)

def _sigmoid(x):
    return jax.nn.sigmoid(x)

def _layernorm(x, axis=-1, eps=1e-05):
    m = jnp.mean(x, axis=axis, keepdims=True)
    v = jnp.var(x, axis=axis, keepdims=True)
    return (x - m) / jnp.sqrt(v + eps)

def _scatter_add(tgt, idx, src, axis=0):
    return tgt.at[idx].add(src)

def _segment_sum(src, seg, n):
    return jax.ops.segment_sum(src, seg, n)
kernel_name = 'mk_adj_preln_d2_adj_r2_643c5d'

def setup_inputs(seed: int=0):
    np.random.seed(seed)
    _w = jnp.asarray

    def _rec_inputs():
        import jax
        import jax.numpy as jnp
        _gk = jax.random.key(seed)
        x = -0.000929 + 1 * jax.random.normal(jax.random.fold_in(_gk, 1), (4096, 128), jnp.float32)
        _w = (1.0 + jnp.arange(4096, dtype=jnp.float32)) ** (-0.5)
        _w = _w / _w.mean()
        _pij = jnp.clip(0.00195312 * _w[:, None] * _w[None, :], 0.0, 1.0)
        _a = jax.random.uniform(jax.random.fold_in(_gk, 2), (4096, 4096)) < _pij
        _a = jnp.logical_or(_a, jnp.eye(4096, dtype=bool))
        _af = _a.astype(jnp.float32)
        _af = _af * jax.random.uniform(jax.random.fold_in(_gk, 3), (4096, 4096), jnp.float32, 0.05, 1)
        adj = _af
        return (x, adj)
    x, adj = _rec_inputs()

    def _L0_gnn_setup():
        import jax, jax.numpy as jnp
        import numpy as np
        N, E, D = (4096, 4096, 128)
        key = jax.random.key(seed)
        k1, k2 = jax.random.split(key)
        X = jax.random.normal(k1, (N, D), dtype=jnp.float32)
        H = jax.random.uniform(k2, (N, E), dtype=jnp.float32)
        return {'X': X, 'H': H}
    _L0_gnn_all = _L0_gnn_setup()
    _L0_gnn_in = {k: v for k, v in _L0_gnn_all.items() if k in ()}
    del _L0_gnn_all

    def _L1_gnn_setup():
        import jax, jax.numpy as jnp
        import numpy as np
        N = 8192
        U = 128
        AVG_DEGREE = 32
        key = jax.random.key(seed)
        kx, ka, kw = jax.random.split(key, 3)
        x = jax.random.normal(kx, (N, U), dtype=jnp.float32)
        adj = (jax.random.uniform(ka, (N, N)) < AVG_DEGREE / N).astype(jnp.float32)
        W = jax.random.normal(kw, (U, U), dtype=jnp.float32) * 0.05
        b = jnp.zeros((U,), dtype=jnp.float32)
        return {'x': x, 'adj': adj, 'W': W, 'b': b}
    _L1_gnn_all = _L1_gnn_setup()
    _L1_gnn_in = {k: v for k, v in _L1_gnn_all.items() if k in ('W', 'b')}
    del _L1_gnn_all
    return {'x': x, 'adj': adj, 'L1_gnn_W': _L1_gnn_in['W'], 'L1_gnn_b': _L1_gnn_in['b']}

def reference(x, adj, L1_gnn_W, L1_gnn_b):
    import jax
    import jax.numpy as jnp

    def _L0_gnn_ref(X, H):
        import jax, jax.numpy as jnp
        import numpy as np
        N, E, D = (4096, 4096, 128)
        msg = jnp.matmul(H.T, X)
        inv_deg = 1.0 / H.sum(axis=0)
        inv_deg = jnp.where(jnp.isinf(inv_deg), 0.0, inv_deg)
        return msg * inv_deg[:, None]

    def _L1_gnn_ref(x, adj, W, b):
        import jax, jax.numpy as jnp
        import numpy as np
        N = 8192
        U = 128
        AVG_DEGREE = 32
        adj = jax.lax.stop_gradient(adj)
        neigh1 = adj @ x
        x1 = jax.nn.swish(neigh1 @ W + b)
        neigh2 = adj @ x1
        x2 = jax.nn.swish(neigh2 @ W + b)
        return x2
    h = jnp.maximum(_layernorm(x, axis=-1), 0.0)
    x = x + _L0_gnn_ref(h, adj)
    h = jnp.maximum(_layernorm(x, axis=-1), 0.0)
    x = x + _L1_gnn_ref(h, adj, L1_gnn_W, L1_gnn_b)
    return x

_drawn_inputs = setup_inputs


def setup_inputs(seed=0):
    import zlib

    import numpy as np

    out = dict(_drawn_inputs(seed))
    spreads = {'L1_gnn_b': (0.0, 0.1)}
    factors = {}
    for name, (base, spread) in spreads.items():
        noise = np.random.default_rng([zlib.crc32(name.encode()), seed]).standard_normal(out[name].shape)
        drawn = base * np.exp(spread * noise) if base else spread * noise
        out[name] = jnp.asarray(drawn.astype(out[name].dtype))
    for name, factor in factors.items():
        out[name] = (out[name] * factor).astype(out[name].dtype)
    return out
```

```python
import concourse.bass as bass
from concourse import mybir
from contextlib import ExitStack

P = 128
N = 4096
NT = N // P
EPS = 1e-5
FLT_MAX = 3.4028234663852886e38

SLAB = 256
SC = SLAB // P
RG = 8
NG = NT // RG
NS = N // SLAB
ITEMS = NS * NG
UNITS = 2
UT = RG // UNITS
RAW = 3
TRING = 6
LAG = 5
BODY = 12
TURNS = (ITEMS - NG) // BODY
POOL_UNITS = {(0, 1), (2, 1)}
HC = 2

GT = 4
N3G = NT // GT
W3 = NT // 2
RAW3 = 4
TRING3 = 4


def build(nc, x_in, adj, w_in, b_in, out):
    f32, f32r = mybir.dt.float32, mybir.dt.float32r
    ALU, ACT, AX = mybir.AluOpType, mybir.ActivationFunctionType, mybir.AxisListType

    x_tiles = x_in.rearrange("(t p) d -> p t d", p=P)
    out_tiles = out.rearrange("(t p) d -> p t d", p=P)
    adj_tiles = adj.rearrange("(t p) c -> p t c", p=P)

    ctx = ExitStack()
    with ctx:
        def sb(name, shape, dt=f32, into=ctx):
            return into.enter_context(nc.sbuf_tensor(name, shape, dt))

        def ps(name, shape):
            return ctx.enter_context(nc.psum_tensor(name, shape, f32))

        def sem(name):
            return ctx.enter_context(nc.semaphore(name))

        x = sb("x", [P, NT, P])
        f_hi = sb("f_hi", [P, NT, P], f32r)
        f_lo = sb("f_lo", [P, NT, P], f32r)
        at_hi = sb("at_hi", [P, TRING * SC, RG * P], f32r)
        at_lo = sb("at_lo", [P, TRING * SC, RG * P], f32r)
        n1T = sb("n1T", [P, N])
        ident = sb("ident", [P, P])
        w = sb("w", [P, P])
        bias = sb("bias", [P, P])
        h2_hi = sb("h2_hi", [P, SC, P], f32r)
        h2_lo = sb("h2_lo", [P, SC, P], f32r)
        msgT = sb("msgT", [P, SLAB])
        u = sb("u", [P, 2, HC, P])
        degp = sb("degp", [P, BODY // NG, SC, NG])
        deg = sb("deg", [P, 5, SC])
        stats = sb("stats", [P, RG, 6])
        mv = sb("mv", [P, HC, 2])
        norm = sb("norm", [P, 4, HC])
        consts = sb("consts", [P, 3])
        mv0 = msgT[:, 0:2 * NT].rearrange("p (t two) -> p t two", two=2)
        norm0 = msgT[:, 2 * NT:6 * NT].rearrange("p (n t) -> p n t", n=4)
        sweep1 = ExitStack()
        raw = sb("raw", [P, RAW, RG, SLAB], into=sweep1)
        a_hi = sb("a_hi", [P, UNITS, UT, SLAB], f32r, into=sweep1)
        a_lo = sb("a_lo", [P, UNITS, UT, SLAB], f32r, into=sweep1)
        sweep1.close()
        raw3 = sb("raw3", [P, RAW3, GT, 4 * P])

        t_ps = ps("t_ps", [P, 2, RG * P])
        p1_ps = ps("p1_ps", [P, 512])
        m_ps = ps("m_ps", [P, 512])
        p2_ps = ps("p2_ps", [P, 2, 512])

        x_loaded = [sem(f"x_loaded{n}") for n in range(4)]
        bias_loaded = sem("bias_loaded")
        consts_ready = sem("consts_ready")
        pool_const = sem("pool_const")
        raw_loaded = [sem(f"raw_loaded{n}") for n in range(RAW)]
        a_hi_ready = sem("a_hi_ready")
        a_lo_dve = sem("a_lo_dve")
        a_lo_pool = sem("a_lo_pool")
        p1_done = sem("p1_done")
        t_done = sem("t_done")
        at_hi_ready = sem("at_hi_ready")
        at_lo_ready = sem("at_lo_ready")
        p2_done = sem("p2_done")
        n1_summed = sem("n1_summed")
        msgT_copied = sem("msgT_copied")
        msg_turned = sem("msg_turned")
        norm_ready = sem("norm_ready")
        u_ready = sem("u_ready")
        mv_ready = sem("mv_ready")
        pool_step = sem("pool_step")
        h_ready = sem("h_ready")
        h2_ready = sem("h2_ready")
        dve_step = sem("dve_step")
        act_step = sem("act_step")
        xw_done = sem("xw_done")
        z_ready = sem("z_ready")
        silu_done = sem("silu_done")
        x1_ready = sem("x1_ready")
        raw3_loaded = [sem(f"raw3_loaded{n}") for n in range(RAW3)]
        t3_done = sem("t3_done")
        at3_hi_ready = sem("at3_hi_ready")
        at3_lo_ready = sem("at3_lo_ready")
        m3_done = sem("m3_done")
        n2_copied = sem("n2_copied")
        y_ready = sem("y_ready")
        w_in_y_out = sem("w_in_y_out")

        block = ctx.enter_context(nc.Block())

        def per_item(i, j, rate, extra=0):
            return i * (BODY * rate) + (rate * j + extra)

        def slab_of(i, j):
            return i * (BODY // NG) + j // NG

        def lo_count(i, j, last_u, pool):
            def mine(g, n):
                return ((g, n) in POOL_UNITS) == pool
            per_slab = sum(mine(g, n) for g in range(NG) for n in range(UNITS))
            here = sum(mine(g, n) for g in range(NG) for n in range(UNITS)
                       if (g, n) <= (j % NG, last_u))
            return i * (per_slab * (BODY // NG)) + (per_slab * (j // NG) + here)

        def wait(eng, s, value):
            if not (isinstance(value, int) and value <= 0):
                eng.wait_ge(s, value)

        def wait_lo(eng, i, j, n):
            if (j % NG, n) in POOL_UNITS:
                eng.wait_ge(a_lo_pool, lo_count(i, j, n, True))
            else:
                eng.wait_ge(a_lo_dve, lo_count(i, j, n, False))

        def first_sweep(eng, item):
            for j in range(NG):
                item(0, j)
            with eng.Fori(0, TURNS) as i:
                for j in range(NG, NG + BODY):
                    item(i, j)

        def second_sweep(eng, group):
            group(0, True, False)
            with eng.Fori(1, N3G - 1) as g:
                group(g, False, False)
            group(N3G - 1, False, True)

        def a_lo_unit(eng, i, j, n, done):
            eng.wait_ge(a_hi_ready, per_item(i, j, UNITS, n + 1))
            src = raw[:, j % RAW, n * UT:(n + 1) * UT, :]
            eng.tensor_tensor(a_lo[:, n], src, a_hi[:, n].bitcast(f32), ALU.subtract).then_inc(done, 1)

        @block.sync
        def _(sp):
            def load(i, j):
                if j >= RAW:
                    sp.wait_ge(p1_done, per_item(i, j - RAW, UNITS, UNITS))
                g = j % NG
                sp.dma_start(raw[:, j % RAW],
                             adj_tiles[:, g * RG:(g + 1) * RG, bass.ds(slab_of(i, j) * SLAB, SLAB)])\
                  .then_inc(raw_loaded[j % RAW], 16)

            first_sweep(sp, load)
            sp.wait_ge(p1_done, ITEMS * UNITS)

            def group(g, first, last):
                for c in range(W3 // 2):
                    if not (first and c < RAW3):
                        sp.wait_ge(t3_done, g * W3 + 2 * (c - RAW3 + 1))
                    sp.dma_start(raw3[:, c % RAW3],
                                 adj_tiles[:, bass.ds(g * GT, GT), c * 4 * P:(c + 1) * 4 * P])\
                      .then_inc(raw3_loaded[c % RAW3], 16)
                    if c == RAW3 and not first:
                        store(g - 1)

            def store(g):
                sp.wait_ge(y_ready, g + 1)
                sp.dma_start(out_tiles[:, bass.ds(g * GT, GT), :],
                             n1T[:, 512:1024].rearrange("p (t d) -> p t d", d=P))\
                  .then_inc(w_in_y_out, 16)

            second_sweep(sp, group)
            store(N3G - 1)
            sp.wait_ge(w_in_y_out, 16 * (N3G + 1))

        @block.tensor
        def _(pe):
            def three(out_ap, hi_w, lo_w, hi_m, lo_m, start, stop):
                pe.matmul(out_ap, hi_w, hi_m, start=start, stop=False)
                pe.matmul(out_ap, hi_w, lo_m, start=False, stop=False)
                return pe.matmul(out_ap, lo_w, hi_m, start=False, stop=stop)

            def transposes(i, j):
                pe.wait_ge(raw_loaded[j % RAW], i * (16 * BODY // RAW) + 16 * (j // RAW + 1))
                for c in range(SC):
                    if j > 0:
                        pe.wait_ge(at_lo_ready, per_item(i, j, SC, SC + c - 1))
                    for t in range(RG):
                        mm = pe.transpose(t_ps[:, c, t * P:(t + 1) * P],
                                          raw[:, j % RAW, t, c * P:(c + 1) * P], ident[:, :])
                    mm.then_inc(t_done, 1)

            def turn_message(i, j):
                pe.wait_ge(msgT_copied, slab_of(i, j))
                for c in range(SC):
                    mm = pe.transpose(m_ps[:, c * P:(c + 1) * P], msgT[:, c * P:(c + 1) * P], ident[:, :])
                mm.then_inc(msg_turned, 1)

            def p1(i, j):
                if j % NG == 0:
                    wait(pe, msgT_copied, slab_of(i, j))
                for n in range(UNITS):
                    if j < NG and isinstance(i, int):
                        pe.wait_ge(h_ready, (j * RG + (n + 1) * UT) // HC)
                    pe.wait_ge(a_hi_ready, per_item(i, j, UNITS, n + 1))
                    wait_lo(pe, i, j, n)
                    for t in range(UT):
                        r = (j % NG) * RG + n * UT + t
                        mm = three(p1_ps[:, 0:SLAB], f_hi[:, r], f_lo[:, r], a_hi[:, n, t], a_lo[:, n, t],
                                   r == 0, r == NT - 1)
                    mm.then_inc(p1_done, 1)

            def p2(i, j, run):
                pe.wait_ge(h2_ready, slab_of(i, j) + 2)
                pe.wait_ge(at_lo_ready, per_item(i, j, SC, 2 * SC))
                pe.wait_ge(n1_summed, run + 1)
                for half in range(2):
                    cols = slice(half * 512, (half + 1) * 512)
                    for c in range(SC):
                        slot = (j % TRING) * SC + c
                        mm = three(p2_ps[:, half, :], h2_hi[:, c], h2_lo[:, c],
                                   at_hi[:, slot, cols], at_lo[:, slot, cols], c == 0, c == SC - 1)
                mm.then_inc(p2_done, 1)

            pe.wait_ge(consts_ready, 1)
            for j in range(NG):
                transposes(0, j)
                p1(0, j)
            with pe.Fori(0, TURNS) as i:
                for j in range(NG, NG + BODY):
                    transposes(i, j)
                    if j % NG == 0:
                        turn_message(i, j)
                    p1(i, j)
                    p2(i, j - LAG, per_item(i, j, 1, -NG))

            def features_w(dst, cols0, done):
                for t in range(GT):
                    mm = pe.matmul(dst[:, t * P:(t + 1) * P], n1T[:, cols0 + t * P:cols0 + (t + 1) * P],
                                   w[:, :], start=True, stop=True)
                mm.then_inc(done, 1)

            def xw(e):
                pe.wait_ge(n1_summed, ITEMS - 1 + e // 2)
                wait(pe, z_ready, e - 1)
                features_w([p1_ps, m_ps][e % 2], e * 512, xw_done)

            def t3(g, j):
                c0 = (j % W3) // 2
                pe.wait_ge(raw3_loaded[c0 % RAW3], g * 32 + 16 * (j // (2 * RAW3) + 1))
                if isinstance(g, int) and g * W3 + j < 2:
                    pe.wait_ge(at_lo_ready, (ITEMS + 1) * SC - 1 + j)
                else:
                    pe.wait_ge(at3_lo_ready, g * W3 + (j - 1))
                for c in range(2):
                    for t in range(GT):
                        mm = pe.transpose(t_ps[:, j % 2, c * 512 + t * P:c * 512 + (t + 1) * P],
                                          raw3[:, c0 % RAW3, t, ((j % 2) * 2 + c) * P:((j % 2) * 2 + c + 1) * P],
                                          ident[:, :])
                mm.then_inc(t3_done, 1)

            def m3(g, j, first):
                pe.wait_ge(at3_lo_ready, g * W3 + (j + 1))
                if first:
                    pe.wait_ge(x1_ready, j // 2 + 1)
                if j == 0 and not first:
                    pe.wait_ge(n2_copied, g)
                for c in range(2):
                    at = slice(c * 512, (c + 1) * 512)
                    mm = three(p2_ps[:, 0, :], f_hi[:, 2 * j + c], f_lo[:, 2 * j + c],
                               at_hi[:, j % TRING3, at], at_lo[:, j % TRING3, at],
                               j == 0 and c == 0, j == W3 - 1 and c == 1)
                mm.then_inc(m3_done, 1)

            def xw3(g):
                pe.wait_ge(n2_copied, g + 1)
                pe.wait_ge(z_ready, g + 8)
                features_w(p1_ps, 0, xw_done)

            pe.wait_ge(w_in_y_out, 16)
            turn_message(0, ITEMS)
            p2(0, ITEMS - LAG, ITEMS - NG)
            for g in range(NG):
                p2(0, ITEMS - NG + g, ITEMS - NG + 1 + g)
                if g >= 1:
                    xw(2 * g - 2)
                    xw(2 * g - 1)
            t3(0, 0)
            t3(0, 1)
            xw(6)
            xw(7)

            def group(g, first, last):
                for j in range(W3):
                    if not (last and j >= W3 - 2):
                        t3(g, j + 2)
                    m3(g, j, first)
                    if j == 2 and not first:
                        xw3(g - 1)

            second_sweep(pe, group)
            xw3(N3G - 1)

        @block.scalar
        def _(act):
            for n in range(4):
                act.dma_start(x[:, n * 8:(n + 1) * 8], x_tiles[:, n * 8:(n + 1) * 8]).then_inc(x_loaded[n], 16)
            act.dma_start(w[:, :], w_in).then_inc(w_in_y_out, 16)
            act.dma_start(bias[:, :], b_in.rearrange("(a d) -> a d", a=1).to_broadcast([P, P])).then_inc(bias_loaded, 16)

            def relu(src, dst, hi, scale_shift):
                for t in range(HC):
                    for to in (dst, hi):
                        ins = act.activation(to[:, t], src[:, t], ACT.Relu, bias=scale_shift[:, 3, t:t + 1],
                                             scale=scale_shift[:, 2, t:t + 1])
                ins.then_inc(u_ready, 1)

            def head(n):
                act.wait_ge(norm_ready, n * HC // RG + 1)
                wait(act, h_ready, n - 1)
                tiles = slice(n * HC, (n + 1) * HC)
                relu(x[:, tiles], u[:, n % 2], f_hi[:, tiles], norm0[:, :, tiles])

            def item(i, j):
                act.wait_ge(raw_loaded[j % RAW], i * (16 * BODY // RAW) + 16 * (j // RAW + 1))
                for n in range(UNITS):
                    wait(act, p1_done, per_item(i, j, UNITS, n + 1 - UNITS))
                    act.activation(a_hi[:, n], raw[:, j % RAW, n * UT:(n + 1) * UT, :], ACT.Copy)\
                       .then_inc(a_hi_ready, 1)
                if j < NG:
                    for n in range(j * RG // HC, (j + 1) * RG // HC):
                        head(n)
                if j >= NG:
                    act.wait_ge(p2_done, per_item(i, j, 1, -NG + 1))
                for c in range(SC):
                    act.wait_ge(t_done, per_item(i, j, SC, c + 1))
                    act.activation(at_hi[:, (j % TRING) * SC + c, :], t_ps[:, c, :], ACT.Copy,
                                   accum_out=degp[:, (j // NG) % (BODY // NG), c, j % NG:j % NG + 1])\
                       .then_inc(at_hi_ready, 1)
                if j % NG == NG - 1:
                    act.wait_ge(p1_done, per_item(i, j, UNITS, UNITS))
                    wait(act, msg_turned, slab_of(i, j))
                    act.activation(msgT[:, :], p1_ps[:, 0:SLAB], ACT.Copy).then_inc(msgT_copied, 1)
                if j % NG == 0 and j > 0:
                    slab_relu(slab_of(i, j), per_item(i, j, 1, -NG + 2))

            def slab_relu(s, p2_before):
                act.wait_ge(norm_ready, s + NG)
                act.wait_ge(h2_ready, s)
                act.wait_ge(p2_done, p2_before)
                relu(u[:, 1], u[:, 0], h2_hi, norm)

            first_sweep(act, item)
            slab_relu(NS, ITEMS - NG + 2)

            act.wait_ge(p1_done, ITEMS * UNITS)
            for e in range(8):
                act.wait_ge(z_ready, e + 1)
                z = n1T[:, e * 512:(e + 1) * 512]
                act.activation(z, z, ACT.Silu).then_inc(act_step, 1)
                act.wait_ge(act_step, e + 1)
                act.activation(f_hi[:, e * GT:(e + 1) * GT], z.rearrange("p (t d) -> p t d", d=P), ACT.Copy)\
                   .then_inc(silu_done, 1)

            def group(g, first, last):
                for j in range(W3):
                    act.wait_ge(t3_done, g * W3 + (j + 1))
                    if first and j < TRING3:
                        act.wait_ge(p2_done, ITEMS)
                    else:
                        act.wait_ge(m3_done, g * W3 + (j - TRING3 + 1))
                    act.activation(at_hi[:, j % TRING3, :], t_ps[:, j % 2, :], ACT.Copy)\
                       .then_inc(at3_hi_ready, 1)
                    if j == 1 and not first:
                        copy_n2(g - 1)
                    if j == 6 and not first:
                        silu3(g - 1)

            def copy_n2(g):
                act.wait_ge(m3_done, (g + 1) * W3)
                act.wait_ge(x1_ready, 8)
                act.wait_ge(xw_done, g + 8)
                act.activation(n1T[:, 0:512], p2_ps[:, 0, :], ACT.Copy).then_inc(n2_copied, 1)

            def silu3(g):
                act.wait_ge(z_ready, g + 9)
                z = n1T[:, 512:1024]
                act.activation(z, z, ACT.Silu).then_inc(silu_done, 1)

            second_sweep(act, group)
            copy_n2(N3G - 1)
            silu3(N3G - 1)

        SLAB_STEPS = 7
        HEAD_STEPS = 1 + NG

        @block.vector
        def _(dve):
            def chained(base):
                count = [0]

                def step(ins):
                    count[0] += 1
                    ins.then_inc(dve_step, 1)
                    dve.wait_ge(dve_step, base + count[0])
                return step, count

            dve.memset(n1T[:, :], 0.0).then_inc(dve_step, 1)
            dve.memset(p2_ps[:, :, :], 0.0).then_inc(p2_done, 1)
            dve.wait_ge(dve_step, 1)

            def statistics(step, src, dst, n):
                for t in range(n):
                    ins = dve.bn_stats(stats[:, t, :], src[:, t])
                step(ins)
                for t in range(n):
                    ins = dve.bn_aggr(dst[:, t, :], stats[:, t, :])
                ins.then_inc(mv_ready, 1)

            head_step, head_count = chained(1)

            def head_statistics(b):
                dve.wait_ge(x_loaded[b], 16)
                wait(dve, mv_ready, b)
                tiles = slice(b * RG, (b + 1) * RG)
                statistics(head_step, x[:, tiles], mv0[:, tiles], RG)

            def head_split(n):
                dve.wait_ge(u_ready, n + 1)
                tiles = slice(n * HC, (n + 1) * HC)
                dve.tensor_tensor(f_lo[:, tiles], u[:, n % 2], f_hi[:, tiles].bitcast(f32), ALU.subtract)\
                   .then_inc(h_ready, 1)

            def slab_norm(i, j):
                s = slab_of(i, j)
                turn = (j // NG - 1) % (BODY // NG)
                step, count = chained((s - 1) * SLAB_STEPS + HEAD_STEPS)
                dve.wait_ge(at_hi_ready, per_item(i, j, SC))
                dve.wait_ge(u_ready, s - 1 + NT // HC)
                total, inv, clamped, finite, inv_deg = (deg[:, n, :] for n in range(5))
                step(dve.tensor_reduce(total, degp[:, turn], AX.X, ALU.add))
                step(dve.reciprocal(inv, total))
                step(dve.tensor_scalar(clamped, inv, -FLT_MAX, FLT_MAX, ALU.max, ALU.min))
                step(dve.tensor_tensor(finite, inv, clamped, ALU.is_equal))
                step(dve.tensor_tensor(inv_deg, clamped, finite, ALU.mult))
                dve.wait_ge(msg_turned, s)
                for c in range(SC):
                    row = x[:, bass.ds((s - 1) * SC + c, 1), :]
                    ins = dve.scalar_tensor_tensor(
                        out=u[:, 1, c:c + 1, :], in0=m_ps[:, c * P:(c + 1) * P].rearrange("p (a d) -> p a d", a=1),
                        scalar=inv_deg[:, c:c + 1], in1=row, op0=ALU.mult, op1=ALU.add)
                step(ins)
                for c in range(SC):
                    ins = dve.bn_stats(stats[:, c, :], u[:, 1, c])
                step(ins)
                dve.tensor_scalar(x[:, bass.ds((s - 1) * SC, SC), :], u[:, 1], 1.0, None, ALU.mult)
                for c in range(SC):
                    ins = dve.bn_aggr(mv[:, c, :], stats[:, c, :])
                ins.then_inc(mv_ready, 1)
                assert count[0] == SLAB_STEPS

            def sum_n1(j, run):
                dve.wait_ge(p2_done, run + 1)
                g = (j - 6) % NG
                rows = n1T[:, g * RG * P:(g + 1) * RG * P]
                dve.tensor_tensor(rows, p2_ps[:, :, :].rearrange("p a b -> p (a b)"), rows, ALU.add)\
                   .then_inc(n1_summed, 1)

            def item(i, j):
                if j == 0:
                    head_statistics(0)
                if j < NG - 1:
                    head_statistics(j + 1)
                for n in range(UNITS):
                    if (j % NG, n) not in POOL_UNITS:
                        a_lo_unit(dve, i, j, n, a_lo_dve)
                if j < NG:
                    for n in range(j * RG // HC, (j + 1) * RG // HC):
                        head_split(n)
                if j >= NG:
                    sum_n1(j, per_item(i, j, 1, -NG))
                for c in range(SC):
                    slot = (j % TRING) * SC + c
                    dve.wait_ge(at_hi_ready, per_item(i, j, SC, c + 1))
                    dve.tensor_tensor(at_lo[:, slot, :], t_ps[:, c, :], at_hi[:, slot, :].bitcast(f32),
                                      ALU.subtract).then_inc(at_lo_ready, 1)
                if j % NG == 0 and j > 0:
                    slab_norm(i, j)

            first_sweep(dve, item)
            slab_norm(0, ITEMS)
            dve.wait_ge(bias_loaded, 16)
            sum_n1(ITEMS, ITEMS - NG)
            sum_n1(ITEMS + 1, ITEMS - NG + 1)

            def add_bias(src, dst, done):
                four = "p (t d) -> p t d"
                dve.tensor_tensor(dst.rearrange(four, d=P), src.rearrange(four, d=P),
                                  bias[:, :].rearrange("p (a d) -> p a d", a=1).to_broadcast([P, GT, P]),
                                  ALU.add).then_inc(done, 1)

            for g in range(NG):
                sum_n1(ITEMS + 2 + g, ITEMS - NG + 2 + g)
                for e in (2 * g, 2 * g + 1):
                    dve.wait_ge(xw_done, e + 1)
                    add_bias([p1_ps, m_ps][e % 2][:, :], n1T[:, e * 512:(e + 1) * 512], z_ready)

            def group(g, first, last):
                for j in range(W3):
                    dve.wait_ge(at3_hi_ready, g * W3 + (j + 1))
                    dve.tensor_tensor(at_lo[:, j % TRING3, :], t_ps[:, j % 2, :],
                                      at_hi[:, j % TRING3, :].bitcast(f32), ALU.subtract)\
                       .then_inc(at3_lo_ready, 1)
                    if j == 5 and not first:
                        bias3(g - 1)
                    if j == 8 and not first:
                        residual(g - 1)

            def bias3(g):
                dve.wait_ge(xw_done, g + 9)
                dve.wait_ge(w_in_y_out, g * 16 + 16)
                add_bias(p1_ps[:, :], n1T[:, 512:1024], z_ready)

            def residual(g):
                dve.wait_ge(silu_done, g + 9)
                y = n1T[:, 512:1024].rearrange("p (t d) -> p t d", d=P)
                dve.tensor_tensor(y, y, x[:, bass.ds(g * GT, GT), :], ALU.add).then_inc(y_ready, 1)

            second_sweep(dve, group)
            bias3(N3G - 1)
            residual(N3G - 1)

        @block.gpsimd
        def _(pool):
            for n, value in enumerate((EPS, -1.0, -0.5)):
                pool.memset(consts[:, n:n + 1], value)
            pool.memset(ident[:, :], 0.0).then_inc(pool_const, 1)
            last = (TRING - 1) * SC
            pool.memset(at_hi[:, last:last + SC, :].bitcast(f32), 0.0)
            pool.memset(at_lo[:, last:last + SC, :].bitcast(f32), 0.0).then_inc(at_lo_ready, SC)
            pool.memset(h2_hi[:, :, :].bitcast(f32), 0.0)
            pool.memset(h2_lo[:, :, :].bitcast(f32), 0.0).then_inc(h2_ready, 1)
            pool.wait_ge(pool_const, 1)
            pool.affine_select(out=ident[:, :], in_=ident[:, :], compare_op=ALU.not_equal, fill=1.0,
                               base=0, pattern=[[-1, P]], channel_multiplier=1).then_inc(consts_ready, 1)

            def scale_shift(stat, dst, n, before):
                eps, minus, power = (consts[:, m:m + 1].to_broadcast([P, n]) for m in range(3))
                pool.tensor_tensor(dst[:, 0], stat[:, :, 1], eps, ALU.add)
                pool.tensor_tensor(dst[:, 1], stat[:, :, 0], minus, ALU.mult).then_inc(pool_step, 1)
                pool.wait_ge(pool_step, before + 1)
                pool.tensor_tensor(dst[:, 2], dst[:, 0], power, ALU.pow).then_inc(pool_step, 1)
                pool.wait_ge(pool_step, before + 2)
                pool.tensor_tensor(dst[:, 3], dst[:, 1], dst[:, 2], ALU.mult).then_inc(norm_ready, 1)

            def head(b):
                pool.wait_ge(mv_ready, b + 1)
                tiles = slice(b * RG, (b + 1) * RG)
                scale_shift(mv0[:, tiles], norm0[:, :, tiles], RG, 2 * b)

            def split_h2(i, j):
                s = slab_of(i, j)
                pool.wait_ge(mv_ready, s + NG)
                scale_shift(mv, norm, HC, (NG + s - 1) * 2)
                pool.wait_ge(u_ready, s + NT // HC)
                pool.tensor_tensor(h2_lo[:, :, :], u[:, 0], h2_hi[:, :, :].bitcast(f32), ALU.subtract)\
                    .then_inc(h2_ready, 1)

            def item(i, j):
                if j == 0:
                    head(0)
                if j < NG - 1:
                    head(j + 1)
                for n in range(UNITS):
                    if (j % NG, n) in POOL_UNITS:
                        a_lo_unit(pool, i, j, n, a_lo_pool)
                if j % NG == 0 and j > 0:
                    split_h2(i, j)

            first_sweep(pool, item)
            split_h2(0, ITEMS)
            for e in range(8):
                pool.wait_ge(silu_done, e + 1)
                at = slice(e * GT, (e + 1) * GT)
                pool.tensor_tensor(f_lo[:, at], n1T[:, e * 512:(e + 1) * 512].rearrange("p (t d) -> p t d", d=P),
                                   f_hi[:, at].bitcast(f32), ALU.subtract).then_inc(x1_ready, 1)


_INS = ["x", "adj", "L1_gnn_W", "L1_gnn_b"]


def kernel(**inputs):
    import numpy as _np
    import concourse.bacc as _bacc
    from concourse import mybir as _mybir
    from concourse.bass_utils import run_bass_kernel_spmd as _run

    nc = _bacc.Bacc("TRN2", target_bir_lowering=False, num_devices=1)
    arrays, args = {}, []
    for name in _INS:
        a = _np.ascontiguousarray(inputs[name])
        arrays[f"in_{name}_dram"] = a
        args.append(nc.dram_tensor(f"in_{name}_dram", a.shape, _mybir.dt.from_np(a.dtype), kind="ExternalInput").ap())
    args.append(nc.dram_tensor("out_dram", (N, P), _mybir.dt.float32, kind="ExternalOutput").ap())
    build(nc, *args)
    r = _run(nc, [arrays], core_ids=[0])
    return r.results[0]["out_dram"]
```

```python
import concourse.bass as bass
from concourse import mybir
from contextlib import ExitStack

P = 128
N = 4096
NT = N // P
EPS = 1e-5
FLT_MAX = 3.4028234663852886e38

SLAB = 256
SC = SLAB // P
RG = 8
NG = NT // RG
NS = N // SLAB
ITEMS = NS * NG
UNITS = 2
UT = RG // UNITS
RAW = 3
TRING = 6
LAG = 5
BODY = 12
TURNS = (ITEMS - NG) // BODY
POOL_UNITS = {(0, 1), (2, 1)}
HC = 2

GT = 4
N3G = NT // GT
SB = 32
QUARTERS = 4
QC = N // QUARTERS
BC = QC // (P // SB)
UC = 2
W3 = NT // UC
WQ = W3 // QUARTERS
RING3 = 4
GROUP = GT * P
EARLY3 = 2
DVE_LO3 = (2, 5, 8, 11, 14)


def build(nc, x_in, adj, w_in, b_in, out):
    f32, f32r = mybir.dt.float32, mybir.dt.float32r
    ALU, ACT, AX = mybir.AluOpType, mybir.ActivationFunctionType, mybir.AxisListType

    x_tiles = x_in.rearrange("(t p) d -> p t d", p=P)
    out_tiles = out.rearrange("(t p) d -> p t d", p=P)
    adj_tiles = adj.rearrange("(t p) c -> p t c", p=P)
    adj_blocks = adj.rearrange("(t p) c -> p t c", p=SB)

    ctx = ExitStack()
    with ctx:
        def sb(name, shape, dt=f32, into=ctx):
            return into.enter_context(nc.sbuf_tensor(name, shape, dt))

        def ps(name, shape):
            return ctx.enter_context(nc.psum_tensor(name, shape, f32))

        def sem(name):
            return ctx.enter_context(nc.semaphore(name))

        x = sb("x", [P, NT, P])
        f_hi = sb("f_hi", [P, NT, P], f32r)
        f_lo = sb("f_lo", [P, NT, P], f32r)
        n1T = sb("n1T", [P, N])
        ident = sb("ident", [P, P])
        w = sb("w", [P, P])
        bias = sb("bias", [P, P])
        h2_hi = sb("h2_hi", [P, SC, P], f32r)
        h2_lo = sb("h2_lo", [P, SC, P], f32r)
        msgT = sb("msgT", [P, SLAB])
        u = sb("u", [P, 2, HC, P])
        degp = sb("degp", [P, BODY // NG, SC, NG])
        deg = sb("deg", [P, 5, SC])
        stats = sb("stats", [P, RG, 6])
        mv = sb("mv", [P, HC, 2])
        norm = sb("norm", [P, 4, HC])
        consts = sb("consts", [P, 3])
        mv0 = msgT[:, 0:2 * NT].rearrange("p (t two) -> p t two", two=2)
        norm0 = msgT[:, 2 * NT:6 * NT].rearrange("p (n t) -> p n t", n=4)
        UNIT = RG * P
        sweep1, sweep2 = ExitStack(), ExitStack()
        at_hi = sb("at_hi", [P, TRING * SC, UNIT], f32r, into=sweep1)
        at_lo = sb("at_lo", [P, TRING * SC, UNIT], f32r, into=sweep1)
        raw = sb("raw", [P, RAW, RG, SLAB], into=sweep1)
        a_hi = sb("a_hi", [P, UNITS, UT, SLAB], f32r, into=sweep1)
        a_lo = sb("a_lo", [P, UNITS, UT, SLAB], f32r, into=sweep1)
        sweep1.close()
        raw3 = {n: sb(f"raw3_{n}", [P, GROUP // SB, BC], into=sweep2) for n in (2, 3)}
        at3_hi = sb("at3_hi", [P, RING3, UC, GROUP], f32r, into=sweep2)
        turned = {n: sb(f"turned{n}", [P, UC, GROUP], into=sweep2) for n in (2, 3)}
        z1 = sb("z1", [P, 2, GROUP], into=sweep2)
        spare = sb("spare", [P, 5, UNIT], into=sweep2)
        at3_lo = sb("at3_lo", [P, RING3, UC, GROUP], f32r, into=sweep2)
        for n in (0, 1):
            raw3[n] = sb(f"raw3_{n}", [P, GROUP // SB, BC], into=sweep2)
        for n in (0, 1):
            turned[n] = sb(f"turned{n}", [P, UC, GROUP], into=sweep2)
        sweep2.close()
        t_ps = ps("t_ps", [P, 2, RG * P])
        p1_ps = ps("p1_ps", [P, 512])
        m_ps = ps("m_ps", [P, 512])
        p2_ps = ps("p2_ps", [P, 2, 512])

        x_loaded = [sem(f"x_loaded{n}") for n in range(4)]
        bias_loaded = sem("bias_loaded")
        consts_ready = sem("consts_ready")
        pool_const = sem("pool_const")
        raw_loaded = [sem(f"raw_loaded{n}") for n in range(RAW)]
        a_hi_ready = sem("a_hi_ready")
        a_lo_dve = sem("a_lo_dve")
        a_lo_pool = sem("a_lo_pool")
        p1_done = sem("p1_done")
        t_done = sem("t_done")
        at_hi_ready = sem("at_hi_ready")
        at_lo_ready = sem("at_lo_ready")
        p2_done = sem("p2_done")
        n1_summed = sem("n1_summed")
        msgT_copied = sem("msgT_copied")
        msg_turned = sem("msg_turned")
        norm_ready = sem("norm_ready")
        u_ready = sem("u_ready")
        mv_ready = sem("mv_ready")
        pool_step = sem("pool_step")
        h_ready = sem("h_ready")
        h2_ready = sem("h2_ready")
        dve_step = sem("dve_step")
        act_step = sem("act_step")
        xw_done = sem("xw_done")
        z_ready = sem("z_ready")
        silu_done = sem("silu_done")
        x1_ready = sem("x1_ready")
        raw3_loaded = [sem(f"raw3_loaded{n}") for n in range(QUARTERS)]
        t3_done = sem("t3_done")
        at3_hi_ready = sem("at3_hi_ready")
        at3_lo_dve = sem("at3_lo_dve")
        at3_lo_pool = sem("at3_lo_pool")
        m3_done = sem("m3_done")
        n2_copied = sem("n2_copied")
        y_ready = sem("y_ready")
        w_in_y_out = sem("w_in_y_out")

        block = ctx.enter_context(nc.Block())

        def per_item(i, j, rate, extra=0):
            return i * (BODY * rate) + (rate * j + extra)

        def slab_of(i, j):
            return i * (BODY // NG) + j // NG

        def lo_count(i, j, last_u, pool):
            def mine(g, n):
                return ((g, n) in POOL_UNITS) == pool
            per_slab = sum(mine(g, n) for g in range(NG) for n in range(UNITS))
            here = sum(mine(g, n) for g in range(NG) for n in range(UNITS)
                       if (g, n) <= (j % NG, last_u))
            return i * (per_slab * (BODY // NG)) + (per_slab * (j // NG) + here)

        def wait(eng, s, value):
            if not (isinstance(value, int) and value <= 0):
                eng.wait_ge(s, value)

        def wait_lo(eng, i, j, n):
            if (j % NG, n) in POOL_UNITS:
                eng.wait_ge(a_lo_pool, lo_count(i, j, n, True))
            else:
                eng.wait_ge(a_lo_dve, lo_count(i, j, n, False))

        def first_sweep(eng, item):
            for j in range(NG):
                item(0, j)
            with eng.Fori(0, TURNS) as i:
                for j in range(NG, NG + BODY):
                    item(i, j)

        def lo3_count(g, j, dve):
            mine = [n for n in range(W3) if (n in DVE_LO3) == dve]
            return g * len(mine) + sum(n <= j for n in mine)

        def ring3_free(eng, g, j):
            if not (isinstance(g, int) and g * W3 + j < RING3):
                eng.wait_ge(m3_done, g * W3 + (j - RING3 + 1))

        def lo3_unit(eng, g, j, done):
            eng.wait_ge(at3_hi_ready, g * W3 + (j + 1))
            eng.tensor_tensor(at3_lo[:, j % RING3], turned[j % RING3][:, :, :],
                              at3_hi[:, j % RING3].bitcast(f32), ALU.subtract).then_inc(done, 1)

        def second_sweep(eng, group):
            group(0, True, False)
            with eng.Fori(1, N3G - 1) as g:
                group(g, False, False)
            group(N3G - 1, False, True)

        def a_lo_unit(eng, i, j, n, done):
            eng.wait_ge(a_hi_ready, per_item(i, j, UNITS, n + 1))
            src = raw[:, j % RAW, n * UT:(n + 1) * UT, :]
            eng.tensor_tensor(a_lo[:, n], src, a_hi[:, n].bitcast(f32), ALU.subtract).then_inc(done, 1)

        @block.sync
        def _(sp):
            def load(i, j):
                if j >= RAW:
                    sp.wait_ge(p1_done, per_item(i, j - RAW, UNITS, UNITS))
                g = j % NG
                sp.dma_start(raw[:, j % RAW],
                             adj_tiles[:, g * RG:(g + 1) * RG, bass.ds(slab_of(i, j) * SLAB, SLAB)])\
                  .then_inc(raw_loaded[j % RAW], 16)

            first_sweep(sp, load)
            def group(g, first, last):
                for q in range(QUARTERS):
                    if first:
                        sp.wait_ge(*[(p1_done, ITEMS * UNITS), (p1_done, ITEMS * UNITS),
                                     (p2_done, 61 + 3), (p2_done, 63 + 3)][q])
                    else:
                        sp.wait_ge(t3_done, g * W3 + WQ * (q + 1 - QUARTERS))
                    for b in range(P // SB):
                        sp.dma_start(raw3[q][b * SB:(b + 1) * SB],
                                     adj_blocks[:, bass.ds(g * (GROUP // SB), GROUP // SB),
                                                q * QC + b * BC:q * QC + (b + 1) * BC])\
                          .then_inc(raw3_loaded[q], 16)
                if not first:
                    store(g - 1)

            def store(g):
                sp.wait_ge(y_ready, g + 1)
                sp.dma_start(out_tiles[:, bass.ds(g * GT, GT), :],
                             n1T[:, 512:1024].rearrange("p (t d) -> p t d", d=P))\
                  .then_inc(w_in_y_out, 16)

            second_sweep(sp, group)
            store(N3G - 1)
            sp.wait_ge(w_in_y_out, 16 * (N3G + 1))

        @block.tensor
        def _(pe):
            def three(out_ap, hi_w, lo_w, hi_m, lo_m, start, stop):
                pe.matmul(out_ap, hi_w, hi_m, start=start, stop=False)
                pe.matmul(out_ap, hi_w, lo_m, start=False, stop=False)
                return pe.matmul(out_ap, lo_w, hi_m, start=False, stop=stop)

            def transposes(i, j):
                pe.wait_ge(raw_loaded[j % RAW], i * (16 * BODY // RAW) + 16 * (j // RAW + 1))
                for c in range(SC):
                    if j > 0:
                        pe.wait_ge(at_lo_ready, per_item(i, j, SC, SC + c - 1))
                    for t in range(RG):
                        mm = pe.transpose(t_ps[:, c, t * P:(t + 1) * P],
                                          raw[:, j % RAW, t, c * P:(c + 1) * P], ident[:, :])
                    mm.then_inc(t_done, 1)

            def turn_message(i, j):
                pe.wait_ge(msgT_copied, slab_of(i, j))
                for c in range(SC):
                    mm = pe.transpose(m_ps[:, c * P:(c + 1) * P], msgT[:, c * P:(c + 1) * P], ident[:, :])
                mm.then_inc(msg_turned, 1)

            def p1(i, j):
                if j % NG == 0:
                    wait(pe, msgT_copied, slab_of(i, j))
                for n in range(UNITS):
                    if j < NG and isinstance(i, int):
                        pe.wait_ge(h_ready, (j * RG + (n + 1) * UT) // HC)
                    pe.wait_ge(a_hi_ready, per_item(i, j, UNITS, n + 1))
                    wait_lo(pe, i, j, n)
                    for t in range(UT):
                        r = (j % NG) * RG + n * UT + t
                        mm = three(p1_ps[:, 0:SLAB], f_hi[:, r], f_lo[:, r], a_hi[:, n, t], a_lo[:, n, t],
                                   r == 0, r == NT - 1)
                    mm.then_inc(p1_done, 1)

            def p2(i, j, run):
                pe.wait_ge(h2_ready, slab_of(i, j) + 2)
                pe.wait_ge(at_lo_ready, per_item(i, j, SC, 2 * SC))
                pe.wait_ge(n1_summed, run + 1)
                for half in range(2):
                    cols = slice(half * 512, (half + 1) * 512)
                    for c in range(SC):
                        slot = (j % TRING) * SC + c
                        mm = three(p2_ps[:, half, :], h2_hi[:, c], h2_lo[:, c],
                                   at_hi[:, slot, cols], at_lo[:, slot, cols], c == 0, c == SC - 1)
                mm.then_inc(p2_done, 1)

            pe.wait_ge(consts_ready, 1)
            for j in range(NG):
                transposes(0, j)
                p1(0, j)
            with pe.Fori(0, TURNS) as i:
                for j in range(NG, NG + BODY):
                    transposes(i, j)
                    if j % NG == 0:
                        turn_message(i, j)
                    p1(i, j)
                    p2(i, j - LAG, per_item(i, j, 1, -NG))

            def features_w(dst, nodes, done):
                for t in range(GT):
                    mm = pe.matmul(dst[:, t * P:(t + 1) * P], nodes(t), w[:, :], start=True, stop=True)
                mm.then_inc(done, 1)

            def xw(e):
                pe.wait_ge(n1_summed, ITEMS - 1 + e // 2)
                wait(pe, z_ready, e - 1)
                features_w([p1_ps, m_ps][e % 2], lambda t: n1T[:, (e * GT + t) * P:(e * GT + t + 1) * P], xw_done)

            def m3(g, j, first):
                if j in DVE_LO3:
                    pe.wait_ge(at3_lo_dve, lo3_count(g, j, True))
                else:
                    pe.wait_ge(at3_lo_pool, lo3_count(g, j, False))
                if first:
                    pe.wait_ge(x1_ready, j // 2 + 1)
                if j == 0 and not first:
                    pe.wait_ge(n2_copied, g)
                for c in range(UC):
                    mm = three(p2_ps[:, 0, :], f_hi[:, UC * j + c], f_lo[:, UC * j + c],
                               at3_hi[:, j % RING3, c], at3_lo[:, j % RING3, c],
                               j == 0 and c == 0, j == W3 - 1 and c == UC - 1)
                mm.then_inc(m3_done, 1)

            def xw3(g):
                pe.wait_ge(n2_copied, g + 1)
                pe.wait_ge(z_ready, g + 8)
                features_w(p1_ps, lambda t: n1T[:, t * P:(t + 1) * P], xw_done)

            pe.wait_ge(w_in_y_out, 16)
            turn_message(0, ITEMS)
            p2(0, ITEMS - LAG, ITEMS - NG)
            for g in range(NG):
                p2(0, ITEMS - NG + g, ITEMS - NG + 1 + g)
                if g >= 1:
                    xw(2 * g - 2)
                    xw(2 * g - 1)
            xw(6)
            xw(7)

            def group(g, first, last):
                for j in range(W3):
                    m3(g, j, first)
                    if j == 2 and not first:
                        xw3(g - 1)

            second_sweep(pe, group)
            xw3(N3G - 1)

        @block.scalar
        def _(act):
            for n in range(4):
                act.dma_start(x[:, n * 8:(n + 1) * 8], x_tiles[:, n * 8:(n + 1) * 8]).then_inc(x_loaded[n], 16)
            act.dma_start(w[:, :], w_in).then_inc(w_in_y_out, 16)
            act.dma_start(bias[:, :], b_in.rearrange("(a d) -> a d", a=1).to_broadcast([P, P])).then_inc(bias_loaded, 16)

            def relu(src, dst, hi, scale_shift):
                for t in range(HC):
                    for to in (dst, hi):
                        ins = act.activation(to[:, t], src[:, t], ACT.Relu, bias=scale_shift[:, 3, t:t + 1],
                                             scale=scale_shift[:, 2, t:t + 1])
                ins.then_inc(u_ready, 1)

            def head(n):
                act.wait_ge(norm_ready, n * HC // RG + 1)
                wait(act, h_ready, n - 1)
                tiles = slice(n * HC, (n + 1) * HC)
                relu(x[:, tiles], u[:, n % 2], f_hi[:, tiles], norm0[:, :, tiles])

            def item(i, j):
                act.wait_ge(raw_loaded[j % RAW], i * (16 * BODY // RAW) + 16 * (j // RAW + 1))
                for n in range(UNITS):
                    wait(act, p1_done, per_item(i, j, UNITS, n + 1 - UNITS))
                    act.activation(a_hi[:, n], raw[:, j % RAW, n * UT:(n + 1) * UT, :], ACT.Copy)\
                       .then_inc(a_hi_ready, 1)
                if j % NG == 1 and j > NG:
                    slab_relu(slab_of(i, j), per_item(i, j - 1, 1, -NG + 2))
                if j < NG:
                    for n in range(j * RG // HC, (j + 1) * RG // HC):
                        head(n)
                if j >= NG:
                    act.wait_ge(p2_done, per_item(i, j, 1, -NG + 1))
                for c in range(SC):
                    act.wait_ge(t_done, per_item(i, j, SC, c + 1))
                    act.activation(at_hi[:, (j % TRING) * SC + c, :], t_ps[:, c, :], ACT.Copy,
                                   accum_out=degp[:, (j // NG) % (BODY // NG), c, j % NG:j % NG + 1])\
                       .then_inc(at_hi_ready, 1)
                if j % NG == NG - 1:
                    act.wait_ge(p1_done, per_item(i, j, UNITS, UNITS))
                    wait(act, msg_turned, slab_of(i, j))
                    act.activation(msgT[:, :], p1_ps[:, 0:SLAB], ACT.Copy).then_inc(msgT_copied, 1)

            def slab_relu(s, p2_before):
                act.wait_ge(norm_ready, s + NG)
                act.wait_ge(h2_ready, s)
                act.wait_ge(p2_done, p2_before)
                relu(u[:, 1], u[:, 0], h2_hi, norm)

            first_sweep(act, item)
            slab_relu(NS, ITEMS - NG + 2)

            act.wait_ge(p1_done, ITEMS * UNITS)
            def x1_hi(e):
                act.wait_ge(z_ready, e + 1)
                z = z1[:, e % 2]
                act.activation(z, z, ACT.Silu).then_inc(act_step, 1)
                act.wait_ge(act_step, e + 1)
                act.activation(f_hi[:, e * GT:(e + 1) * GT], z.rearrange("p (t d) -> p t d", d=P), ACT.Copy)\
                   .then_inc(silu_done, 1)

            def hi3(g, j):
                act.wait_ge(t3_done, g * W3 + (j + 1))
                ring3_free(act, g, j)
                act.activation(at3_hi[:, j % RING3], turned[j % RING3][:, :, :], ACT.Copy)\
                   .then_inc(at3_hi_ready, 1)

            for e in range(4):
                x1_hi(e)
            for j in range(EARLY3):
                hi3(0, j)
            for e in range(4, 8):
                x1_hi(e)

            def group(g, first, last):
                for j in range(EARLY3 if first else 0, W3):
                    hi3(g, j)
                    if j == 1 and not first:
                        copy_n2(g - 1)
                    if j == 6 and not first:
                        silu3(g - 1)

            def copy_n2(g):
                act.wait_ge(m3_done, (g + 1) * W3)
                act.wait_ge(x1_ready, 8)
                act.wait_ge(xw_done, g + 8)
                act.activation(n1T[:, 0:512], p2_ps[:, 0, :], ACT.Copy).then_inc(n2_copied, 1)

            def silu3(g):
                act.wait_ge(z_ready, g + 9)
                z = n1T[:, 512:1024]
                act.activation(z, z, ACT.Silu).then_inc(silu_done, 1)

            second_sweep(act, group)
            copy_n2(N3G - 1)
            silu3(N3G - 1)

        SLAB_STEPS = 7
        HEAD_STEPS = 1 + NG

        @block.vector
        def _(dve):
            def chained(base):
                count = [0]

                def step(ins, between=lambda: None):
                    count[0] += 1
                    ins.then_inc(dve_step, 1)
                    between()
                    dve.wait_ge(dve_step, base + count[0])
                return step, count

            dve.memset(n1T[:, :], 0.0).then_inc(dve_step, 1)
            dve.memset(p2_ps[:, :, :], 0.0).then_inc(p2_done, 1)
            dve.wait_ge(dve_step, 1)

            def statistics(step, src, dst, n):
                for t in range(n):
                    ins = dve.bn_stats(stats[:, t, :], src[:, t])
                step(ins)
                for t in range(n):
                    ins = dve.bn_aggr(dst[:, t, :], stats[:, t, :])
                ins.then_inc(mv_ready, 1)

            head_step, head_count = chained(1)

            def head_statistics(b):
                dve.wait_ge(x_loaded[b], 16)
                wait(dve, mv_ready, b)
                tiles = slice(b * RG, (b + 1) * RG)
                statistics(head_step, x[:, tiles], mv0[:, tiles], RG)

            def head_split(n):
                dve.wait_ge(u_ready, n + 1)
                tiles = slice(n * HC, (n + 1) * HC)
                dve.tensor_tensor(f_lo[:, tiles], u[:, n % 2], f_hi[:, tiles].bitcast(f32), ALU.subtract)\
                   .then_inc(h_ready, 1)

            def slab_norm(i, j, work):
                s = slab_of(i, j)
                turn = (j // NG - 1) % (BODY // NG)
                chain, count = chained((s - 1) * SLAB_STEPS + HEAD_STEPS)

                def step(ins, n=None):
                    chain(ins, (lambda: work(n)) if n is not None else lambda: None)

                dve.wait_ge(at_hi_ready, per_item(i, j, SC))
                dve.wait_ge(u_ready, s - 1 + NT // HC)
                total, inv, clamped, finite, inv_deg = (deg[:, n, :] for n in range(5))
                step(dve.tensor_reduce(total, degp[:, turn], AX.X, ALU.add), 0)
                step(dve.reciprocal(inv, total), 1)
                step(dve.tensor_scalar(clamped, inv, -FLT_MAX, FLT_MAX, ALU.max, ALU.min), 2)
                step(dve.tensor_tensor(finite, inv, clamped, ALU.is_equal), 3)
                step(dve.tensor_tensor(inv_deg, clamped, finite, ALU.mult), 4)
                dve.wait_ge(msg_turned, s)
                for c in range(SC):
                    row = x[:, bass.ds((s - 1) * SC + c, 1), :]
                    ins = dve.scalar_tensor_tensor(
                        out=u[:, 1, c:c + 1, :], in0=m_ps[:, c * P:(c + 1) * P].rearrange("p (a d) -> p a d", a=1),
                        scalar=inv_deg[:, c:c + 1], in1=row, op0=ALU.mult, op1=ALU.add)
                step(ins)
                for c in range(SC):
                    ins = dve.bn_stats(stats[:, c, :], u[:, 1, c])
                step(ins)
                dve.tensor_scalar(x[:, bass.ds((s - 1) * SC, SC), :], u[:, 1], 1.0, None, ALU.mult)
                for c in range(SC):
                    ins = dve.bn_aggr(mv[:, c, :], stats[:, c, :])
                ins.then_inc(mv_ready, 1)
                assert count[0] == SLAB_STEPS

            def sum_n1(j, run):
                dve.wait_ge(p2_done, run + 1)
                g = (j - 6) % NG
                rows = n1T[:, g * QC:(g + 1) * QC].rearrange("p (m b c) -> p b m c", b=P // SB, c=SB)
                new = p2_ps[:, :, :].rearrange("p h n -> p (h n)").rearrange("p (b m c) -> p b m c", b=P // SB, c=SB)
                dve.tensor_tensor(rows, new, rows, ALU.add)\
                   .then_inc(n1_summed, 1)

            def item(i, j):
                if j == 0:
                    head_statistics(0)
                if j < NG - 1:
                    head_statistics(j + 1)
                def work(n):
                    if n < UNITS and (j % NG, n) not in POOL_UNITS:
                        a_lo_unit(dve, i, j, n, a_lo_dve)
                    if n == UNITS and j < NG:
                        for chunk in range(j * RG // HC, (j + 1) * RG // HC):
                            head_split(chunk)
                    if n == UNITS and j >= NG:
                        sum_n1(j, per_item(i, j, 1, -NG))
                    if n > UNITS:
                        c = n - UNITS - 1
                        slot = (j % TRING) * SC + c
                        dve.wait_ge(at_hi_ready, per_item(i, j, SC, c + 1))
                        dve.tensor_tensor(at_lo[:, slot, :], t_ps[:, c, :], at_hi[:, slot, :].bitcast(f32),
                                          ALU.subtract).then_inc(at_lo_ready, 1)

                if j % NG == 0 and j > 0:
                    slab_norm(i, j, work)
                else:
                    for n in range(UNITS + 1 + SC):
                        work(n)

            first_sweep(dve, item)
            slab_norm(0, ITEMS, lambda n: None)
            dve.wait_ge(bias_loaded, 16)
            sum_n1(ITEMS, ITEMS - NG)
            sum_n1(ITEMS + 1, ITEMS - NG + 1)

            def add_bias(src, dst, done):
                four = "p (t d) -> p t d"
                dve.tensor_tensor(dst.rearrange(four, d=P), src.rearrange(four, d=P),
                                  bias[:, :].rearrange("p (a d) -> p a d", a=1).to_broadcast([P, GT, P]),
                                  ALU.add).then_inc(done, 1)

            def turn3(g, j):
                if j % WQ == 0:
                    dve.wait_ge(raw3_loaded[j // WQ], (g + 1) * 16 * (P // SB))
                if isinstance(g, int) and g == 0 and j == 2:
                    dve.wait_ge(p2_done, 63 + 3)
                ring3_free(dve, g, j)
                m = (j % WQ) * UC
                src = raw3[j // WQ][:, :, m * SB:(m + UC) * SB].rearrange("p t (m c) -> p m t c", c=SB)
                dst = turned[j % RING3][:, :, :].rearrange("p m (t r) -> p m t r", r=SB)
                dve.transpose(dst, src).then_inc(t3_done, 1)

            for g in range(NG):
                sum_n1(ITEMS + 2 + g, ITEMS - NG + 2 + g)
                if g == NG - 2:
                    for j in range(EARLY3):
                        turn3(0, j)
                if g == 0:
                    dve.wait_ge(p2_done, 61 + 3)
                for e in (2 * g, 2 * g + 1):
                    dve.wait_ge(xw_done, e + 1)
                    wait(dve, x1_ready, e - 1)
                    add_bias([p1_ps, m_ps][e % 2][:, :], z1[:, e % 2], z_ready)

            def group(g, first, last):
                for j in range(EARLY3 if first else 0, W3):
                    turn3(g, j)
                    if j - 1 in DVE_LO3:
                        lo3_unit(dve, g, j - 1, at3_lo_dve)
                    if j == 5 and not first:
                        bias3(g - 1)
                    if j == 9 and not first:
                        residual(g - 1)

            def bias3(g):
                dve.wait_ge(xw_done, g + 9)
                dve.wait_ge(w_in_y_out, g * 16 + 16)
                add_bias(p1_ps[:, :], n1T[:, 512:1024], z_ready)

            def residual(g):
                dve.wait_ge(silu_done, g + 9)
                y = n1T[:, 512:1024].rearrange("p (t d) -> p t d", d=P)
                dve.tensor_tensor(y, y, x[:, bass.ds(g * GT, GT), :], ALU.add).then_inc(y_ready, 1)

            second_sweep(dve, group)
            bias3(N3G - 1)
            residual(N3G - 1)

        @block.gpsimd
        def _(pool):
            for n, value in enumerate((EPS, -1.0, -0.5)):
                pool.memset(consts[:, n:n + 1], value)
            pool.memset(ident[:, :], 0.0).then_inc(pool_const, 1)
            last = (TRING - 1) * SC
            pool.memset(at_hi[:, last:last + SC, :].bitcast(f32), 0.0)
            pool.memset(at_lo[:, last:last + SC, :].bitcast(f32), 0.0).then_inc(at_lo_ready, SC)
            pool.memset(h2_hi[:, :, :].bitcast(f32), 0.0)
            pool.memset(h2_lo[:, :, :].bitcast(f32), 0.0).then_inc(h2_ready, 1)
            pool.wait_ge(pool_const, 1)
            pool.affine_select(out=ident[:, :], in_=ident[:, :], compare_op=ALU.not_equal, fill=1.0,
                               base=0, pattern=[[-1, P]], channel_multiplier=1).then_inc(consts_ready, 1)

            def scale_shift(stat, dst, n, before):
                eps, minus, power = (consts[:, m:m + 1].to_broadcast([P, n]) for m in range(3))
                pool.tensor_tensor(dst[:, 0], stat[:, :, 1], eps, ALU.add)
                pool.tensor_tensor(dst[:, 1], stat[:, :, 0], minus, ALU.mult).then_inc(pool_step, 1)
                pool.wait_ge(pool_step, before + 1)
                pool.tensor_tensor(dst[:, 2], dst[:, 0], power, ALU.pow).then_inc(pool_step, 1)
                pool.wait_ge(pool_step, before + 2)
                pool.tensor_tensor(dst[:, 3], dst[:, 1], dst[:, 2], ALU.mult).then_inc(norm_ready, 1)

            def head(b):
                pool.wait_ge(mv_ready, b + 1)
                tiles = slice(b * RG, (b + 1) * RG)
                scale_shift(mv0[:, tiles], norm0[:, :, tiles], RG, 2 * b)

            def split_h2(i, j):
                s = slab_of(i, j)
                pool.wait_ge(mv_ready, s + NG)
                scale_shift(mv, norm, HC, (NG + s - 1) * 2)
                pool.wait_ge(u_ready, s + NT // HC)
                pool.tensor_tensor(h2_lo[:, :, :], u[:, 0], h2_hi[:, :, :].bitcast(f32), ALU.subtract)\
                    .then_inc(h2_ready, 1)

            def item(i, j):
                if j == 0:
                    head(0)
                if j < NG - 1:
                    head(j + 1)
                for n in range(UNITS):
                    if (j % NG, n) in POOL_UNITS:
                        a_lo_unit(pool, i, j, n, a_lo_pool)
                if j % NG == 0 and j > 0:
                    split_h2(i, j)

            first_sweep(pool, item)
            split_h2(0, ITEMS)
            def x1_lo(e):
                pool.wait_ge(silu_done, e + 1)
                at = slice(e * GT, (e + 1) * GT)
                pool.tensor_tensor(f_lo[:, at], z1[:, e % 2].rearrange("p (t d) -> p t d", d=P),
                                   f_hi[:, at].bitcast(f32), ALU.subtract).then_inc(x1_ready, 1)

            for e in range(8):
                x1_lo(e)

            def group(g, first, last):
                for j in range(W3):
                    if j not in DVE_LO3:
                        lo3_unit(pool, g, j, at3_lo_pool)

            second_sweep(pool, group)


_INS = ["x", "adj", "L1_gnn_W", "L1_gnn_b"]


def kernel(**inputs):
    import numpy as _np
    import concourse.bacc as _bacc
    from concourse import mybir as _mybir
    from concourse.bass_utils import run_bass_kernel_spmd as _run

    nc = _bacc.Bacc("TRN2", target_bir_lowering=False, num_devices=1)
    arrays, args = {}, []
    for name in _INS:
        a = _np.ascontiguousarray(inputs[name])
        arrays[f"in_{name}_dram"] = a
        args.append(nc.dram_tensor(f"in_{name}_dram", a.shape, _mybir.dt.from_np(a.dtype), kind="ExternalInput").ap())
    args.append(nc.dram_tensor("out_dram", (N, P), _mybir.dt.float32, kind="ExternalOutput").ap())
    build(nc, *args)
    r = _run(nc, [arrays], core_ids=[0])
    return r.results[0]["out_dram"]
```

```python
import concourse.bass as bass
from concourse import mybir
from contextlib import ExitStack

P = 128
N = 4096
NT = N // P
EPS = 1e-5
FLT_MAX = 3.4028234663852886e38

SLAB = 256
SC = SLAB // P
RG = 8
NG = NT // RG
NS = N // SLAB
ITEMS = NS * NG
UNITS = 2
UT = RG // UNITS
RAW = 3
TRING = 6
LAG = 5
BODY = 12
TURNS = (ITEMS - NG) // BODY
POOL_UNITS = {(0, 1), (2, 1)}
HC = 2

GT = 4
N3G = NT // GT
SB = 32
QUARTERS = 4
QC = N // QUARTERS
BC = QC // (P // SB)
UC = 2
W3 = NT // UC
WQ = W3 // QUARTERS
TURNED3 = 8
RING3 = 4
GROUP = GT * P
EARLY3 = 2
WHOLE3 = (3, 7, 11, 14)
POOL_ROWS = 400


def build(nc, x_in, adj, w_in, b_in, out):
    f32, f32r = mybir.dt.float32, mybir.dt.float32r
    ALU, ACT, AX = mybir.AluOpType, mybir.ActivationFunctionType, mybir.AxisListType

    x_tiles = x_in.rearrange("(t p) d -> p t d", p=P)
    out_tiles = out.rearrange("(t p) d -> p t d", p=P)
    adj_tiles = adj.rearrange("(t p) c -> p t c", p=P)
    adj_blocks = adj.rearrange("(t p) c -> p t c", p=SB)

    ctx = ExitStack()
    with ctx:
        def sb(name, shape, dt=f32, into=ctx):
            return into.enter_context(nc.sbuf_tensor(name, shape, dt))

        def ps(name, shape):
            return ctx.enter_context(nc.psum_tensor(name, shape, f32))

        def sem(name):
            return ctx.enter_context(nc.semaphore(name))

        x = sb("x", [P, NT, P])
        f_hi = sb("f_hi", [P, NT, P], f32r)
        f_lo = sb("f_lo", [P, NT, P], f32r)
        n1T = sb("n1T", [P, N])
        ident = sb("ident", [P, P])
        w = sb("w", [P, P])
        bias = sb("bias", [P, P])
        h2_hi = sb("h2_hi", [P, SC, P], f32r)
        h2_lo = sb("h2_lo", [P, SC, P], f32r)
        msgT = sb("msgT", [P, SLAB])
        u = sb("u", [P, 2, HC, P])
        degp = sb("degp", [P, BODY // NG, SC, NG])
        deg = sb("deg", [P, 5, SC])
        stats = sb("stats", [P, RG, 6])
        mv = sb("mv", [P, HC, 2])
        norm = sb("norm", [P, 4, HC])
        consts = sb("consts", [P, 3])
        mv0 = msgT[:, 0:2 * NT].rearrange("p (t two) -> p t two", two=2)
        norm0 = msgT[:, 2 * NT:6 * NT].rearrange("p (n t) -> p n t", n=4)
        h_rows = n1T[:, :].rearrange("p (t d) -> p t d", d=P)
        UNIT = RG * P
        sweep1, sweep2 = ExitStack(), ExitStack()
        at_hi = sb("at_hi", [P, TRING * SC, UNIT], f32r, into=sweep1)
        at_lo = sb("at_lo", [P, TRING * SC, UNIT], f32r, into=sweep1)
        raw = sb("raw", [P, RAW, RG, SLAB], into=sweep1)
        a_hi = sb("a_hi", [P, UNITS, UT, SLAB], f32r, into=sweep1)
        a_lo = sb("a_lo", [P, UNITS, UT, SLAB], f32r, into=sweep1)
        sweep1.close()
        raw3 = {n: sb(f"raw3_{n}", [P, GROUP // SB, BC], into=sweep2) for n in (2, 3)}
        at3_hi = sb("at3_hi", [P, RING3, UC, GROUP], f32r, into=sweep2)
        turned = {n: sb(f"turned{n}", [P, UC, GROUP], into=sweep2) for n in range(2, TURNED3)}
        tail = sb("tail", [P, 3, GROUP], into=sweep2)
        spare = sb("spare", [P, GROUP], into=sweep2)
        at3_lo = sb("at3_lo", [P, RING3, UC, GROUP], f32r, into=sweep2)
        for n in (0, 1):
            raw3[n] = sb(f"raw3_{n}", [P, GROUP // SB, BC], into=sweep2)
        for n in (0, 1):
            turned[n] = sb(f"turned{n}", [P, UC, GROUP], into=sweep2)
        sweep2.close()
        t_ps = ps("t_ps", [P, 2, RG * P])
        p1_ps = ps("p1_ps", [P, 512])
        m_ps = ps("m_ps", [P, 512])
        p2_ps = ps("p2_ps", [P, 2, 512])

        x_loaded = [sem(f"x_loaded{n}") for n in range(4)]
        consts_ready = sem("consts_ready")
        pool_const = sem("pool_const")
        raw_loaded = [sem(f"raw_loaded{n}") for n in range(RAW)]
        a_hi_ready = sem("a_hi_ready")
        a_lo_dve = sem("a_lo_dve")
        a_lo_pool = sem("a_lo_pool")
        p1_done = sem("p1_done")
        t_done = sem("t_done")
        at_hi_ready = sem("at_hi_ready")
        at_lo_ready = sem("at_lo_ready")
        p2_done = sem("p2_done")
        n1_summed = sem("n1_summed")
        msgT_copied = sem("msgT_copied")
        msg_turned = sem("msg_turned")
        norm_ready = sem("norm_ready")
        u_ready = sem("u_ready")
        mv_ready = sem("mv_ready")
        pool_step = sem("pool_step")
        h_hi_ready = sem("h_hi_ready")
        h_ready = sem("h_ready")
        n1_zeroed = sem("n1_zeroed")
        h2_ready = sem("h2_ready")
        dve_step = sem("dve_step")
        act_step = sem("act_step")
        xw_done = sem("xw_done")
        z_ready = sem("z_ready")
        silu_done = sem("silu_done")
        x1_ready = sem("x1_ready")
        raw3_loaded = [sem(f"raw3_loaded{n}") for n in range(QUARTERS)]
        t3_done = sem("t3_done")
        at3_hi_ready = sem("at3_hi_ready")
        at3_lo_dve = sem("at3_lo_dve")
        at3_lo_pool = sem("at3_lo_pool")
        m3_done = sem("m3_done")
        n2_copied = sem("n2_copied")
        y_ready = sem("y_ready")
        y_out = [sem("w_in_y_out"), sem("b_in_y_out")]

        block = ctx.enter_context(nc.Block())

        def per_item(i, j, rate, extra=0):
            return i * (BODY * rate) + (rate * j + extra)

        def slab_of(i, j):
            return i * (BODY // NG) + j // NG

        def lo_count(i, j, last_u, pool):
            def mine(g, n):
                return ((g, n) in POOL_UNITS) == pool
            per_slab = sum(mine(g, n) for g in range(NG) for n in range(UNITS))
            here = sum(mine(g, n) for g in range(NG) for n in range(UNITS)
                       if (g, n) <= (j % NG, last_u))
            return i * (per_slab * (BODY // NG)) + (per_slab * (j // NG) + here)

        def wait(eng, s, value):
            if not (isinstance(value, int) and value <= 0):
                eng.wait_ge(s, value)

        def wait_lo(eng, i, j, n):
            if (j % NG, n) in POOL_UNITS:
                eng.wait_ge(a_lo_pool, lo_count(i, j, n, True))
            else:
                eng.wait_ge(a_lo_dve, lo_count(i, j, n, False))

        def first_sweep(eng, item):
            for j in range(NG):
                item(0, j)
            with eng.Fori(0, TURNS) as i:
                for j in range(NG, NG + BODY):
                    item(i, j)

        def split_count(g, j):
            return g * (W3 - len(WHOLE3)) + sum(n <= j and n not in WHOLE3 for n in range(W3))

        def turned_free(eng, g, j):
            if isinstance(g, int) and g * W3 + j < TURNED3:
                return
            back = (j - TURNED3) % W3
            if back in WHOLE3:
                eng.wait_ge(m3_done, g * W3 + (j - TURNED3 + 1))
            else:
                used = split_count(g, j - TURNED3) if j >= TURNED3 else split_count(g - 1, back)
                eng.wait_ge(at3_lo_dve, used)
                eng.wait_ge(at3_lo_pool, used)

        def lo3_part(eng, g, j, rows, done):
            eng.wait_ge(at3_hi_ready, split_count(g, j))
            eng.tensor_tensor(at3_lo[:, j % RING3, :, rows], turned[j % TURNED3][:, :, rows],
                              at3_hi[:, j % RING3, :, rows].bitcast(f32), ALU.subtract).then_inc(done, 1)

        def second_sweep(eng, group):
            group(0, 0, True)
            with eng.Fori(1, N3G - 1, 2) as g:
                group(g, 1, False)
                group(g + 1, 0, False)
            group(N3G - 1, 1, False)

        def a_lo_unit(eng, i, j, n, done):
            eng.wait_ge(a_hi_ready, per_item(i, j, UNITS, n + 1))
            src = raw[:, j % RAW, n * UT:(n + 1) * UT, :]
            eng.tensor_tensor(a_lo[:, n], src, a_hi[:, n].bitcast(f32), ALU.subtract).then_inc(done, 1)

        @block.sync
        def _(sp):
            def load(i, j):
                if j >= RAW:
                    sp.wait_ge(p1_done, per_item(i, j - RAW, UNITS, UNITS))
                g = j % NG
                sp.dma_start(raw[:, j % RAW],
                             adj_tiles[:, g * RG:(g + 1) * RG, bass.ds(slab_of(i, j) * SLAB, SLAB)])\
                  .then_inc(raw_loaded[j % RAW], 16)

            for j in range(NG):
                rows = slice(j * RG, (j + 1) * RG)
                sp.dma_start(x[:, rows], x_tiles[:, rows]).then_inc(x_loaded[j], 16)
                if j < RAW:
                    load(0, j)
            load(0, RAW)
            with sp.Fori(0, TURNS) as i:
                for j in range(NG, NG + BODY):
                    load(i, j)
            def group(g, parity, first):
                for q in range(QUARTERS):
                    if first:
                        sp.wait_ge(*[(p1_done, ITEMS * UNITS), (p1_done, ITEMS * UNITS),
                                     (p2_done, 61 + 3), (p2_done, 63 + 3)][q])
                    else:
                        sp.wait_ge(t3_done, g * W3 + WQ * (q + 1 - QUARTERS))
                    for b in range(P // SB):
                        sp.dma_start(raw3[q][b * SB:(b + 1) * SB],
                                     adj_blocks[:, bass.ds(g * (GROUP // SB), GROUP // SB),
                                                q * QC + b * BC:q * QC + (b + 1) * BC])\
                          .then_inc(raw3_loaded[q], 16)
            second_sweep(sp, group)

        @block.tensor
        def _(pe):
            def three(out_ap, hi_w, lo_w, hi_m, lo_m, start, stop):
                pe.matmul(out_ap, hi_w, hi_m, start=start, stop=False)
                pe.matmul(out_ap, hi_w, lo_m, start=False, stop=False)
                return pe.matmul(out_ap, lo_w, hi_m, start=False, stop=stop)

            def transposes(i, j):
                pe.wait_ge(raw_loaded[j % RAW], i * (16 * BODY // RAW) + 16 * (j // RAW + 1))
                for c in range(SC):
                    if j > 0:
                        pe.wait_ge(at_lo_ready, per_item(i, j, SC, SC + c - 1))
                    for t in range(RG):
                        mm = pe.transpose(t_ps[:, c, t * P:(t + 1) * P],
                                          raw[:, j % RAW, t, c * P:(c + 1) * P], ident[:, :])
                    mm.then_inc(t_done, 1)

            def turn_message(i, j):
                pe.wait_ge(msgT_copied, slab_of(i, j))
                for c in range(SC):
                    mm = pe.transpose(m_ps[:, c * P:(c + 1) * P], msgT[:, c * P:(c + 1) * P], ident[:, :])
                mm.then_inc(msg_turned, 1)

            def p1(i, j):
                if j % NG == 0:
                    wait(pe, msgT_copied, slab_of(i, j))
                for n in range(UNITS):
                    if j < NG and isinstance(i, int):
                        pe.wait_ge(h_ready, j * UNITS + n + 1)
                    pe.wait_ge(a_hi_ready, per_item(i, j, UNITS, n + 1))
                    wait_lo(pe, i, j, n)
                    for t in range(UT):
                        r = (j % NG) * RG + n * UT + t
                        mm = three(p1_ps[:, 0:SLAB], f_hi[:, r], f_lo[:, r], a_hi[:, n, t], a_lo[:, n, t],
                                   r == 0, r == NT - 1)
                    mm.then_inc(p1_done, 1)

            def p2(i, j, run, dst=p2_ps, back=1):
                pe.wait_ge(h2_ready, slab_of(i, j) + 2)
                pe.wait_ge(at_lo_ready, per_item(i, j, SC, 2 * SC))
                pe.wait_ge(n1_summed, run + 2 - back)
                halves = dst if dst is p2_ps else dst.rearrange("p (h n) -> p h n", h=2)
                for half in range(2):
                    cols = slice(half * 512, (half + 1) * 512)
                    for c in range(SC):
                        slot = (j % TRING) * SC + c
                        mm = three(halves[:, half], h2_hi[:, c], h2_lo[:, c],
                                   at_hi[:, slot, cols], at_lo[:, slot, cols], c == 0, c == SC - 1)
                mm.then_inc(p2_done, 1)

            pe.wait_ge(consts_ready, 1)
            for j in range(NG):
                transposes(0, j)
                p1(0, j)
            with pe.Fori(0, TURNS) as i:
                for j in range(NG, NG + BODY):
                    transposes(i, j)
                    if j % NG == 0:
                        turn_message(i, j)
                    p1(i, j)
                    p2(i, j - LAG, per_item(i, j, 1, -NG))

            def features_w(dst, nodes, done):
                for t in range(GT):
                    mm = pe.matmul(dst[:, t * P:(t + 1) * P], nodes(t), w[:, :], start=True, stop=True)
                mm.then_inc(done, 1)

            def xw(e):
                pe.wait_ge(n1_summed, ITEMS - 1 + e // 2)
                wait(pe, z_ready, e - 1)
                features_w([p1_ps, m_ps][e % 2], lambda t: n1T[:, (e * GT + t) * P:(e * GT + t + 1) * P], xw_done)

            def m3(g, parity, j, first):
                if first:
                    pe.wait_ge(x1_ready, j // 2 + 1)
                acc, start, stop = p2_ps[:, parity, :], j == 0, j == W3 - 1
                if j in WHOLE3:
                    pe.wait_ge(t3_done, g * W3 + (j + 1))
                    for c in range(UC):
                        mm = pe.matmul(acc, n1T[:, (UC * j + c) * P:(UC * j + c + 1) * P],
                                       turned[j % TURNED3][:, c], start=False, stop=False)
                else:
                    pe.wait_ge(at3_hi_ready, split_count(g, j))
                    for c in range(UC):
                        pe.matmul(acc, f_hi[:, UC * j + c], at3_hi[:, j % RING3, c],
                                  start=start and c == 0, stop=False)
                        pe.matmul(acc, f_lo[:, UC * j + c], at3_hi[:, j % RING3, c], start=False, stop=False)
                    pe.wait_ge(at3_lo_dve, split_count(g, j))
                    pe.wait_ge(at3_lo_pool, split_count(g, j))
                    for c in range(UC):
                        mm = pe.matmul(acc, f_hi[:, UC * j + c], at3_lo[:, j % RING3, c],
                                       start=False, stop=stop and c == UC - 1)
                mm.then_inc(m3_done, 1)

            def xw3(g):
                pe.wait_ge(n2_copied, g + 1)
                pe.wait_ge(z_ready, g + 8)
                features_w(p1_ps, lambda t: tail[:, 0, t * P:(t + 1) * P], xw_done)

            pe.wait_ge(y_out[0], 16)
            turn_message(0, ITEMS)
            p2(0, ITEMS - LAG, ITEMS - NG)
            pe.wait_ge(at_lo_ready, (ITEMS + 1) * SC)
            for g in range(NG):
                p2(0, ITEMS - NG + g, ITEMS - NG + 1 + g, dst=[t_ps[:, 0, :], p2_ps][g % 2], back=2)
                if g >= 1:
                    xw(2 * g - 2)
                    xw(2 * g - 1)
            xw(6)
            xw(7)

            def group(g, parity, first):
                for j in range(W3):
                    m3(g, parity, j, first)
                    if j == 2 and not first:
                        xw3(g - 1)

            second_sweep(pe, group)
            xw3(N3G - 1)

        @block.scalar
        def _(act):
            act.dma_start(w[:, :], w_in).then_inc(y_out[0], 16)
            act.dma_start(bias[:, :], b_in.rearrange("(a d) -> a d", a=1).to_broadcast([P, P])).then_inc(y_out[1], 16)

            def relu(src, dst, hi, scale_shift):
                for t in range(HC):
                    for to in (dst,) if hi is None else (dst, hi):
                        ins = act.activation(to[:, t], src[:, t], ACT.Relu, bias=scale_shift[:, 3, t:t + 1],
                                             scale=scale_shift[:, 2, t:t + 1])
                ins.then_inc(u_ready, 1)

            def head(n):
                act.wait_ge(norm_ready, n * HC // RG + 1)
                tiles = slice(n * HC, (n + 1) * HC)
                relu(x[:, tiles], h_rows[:, tiles], None, norm0[:, :, tiles])

            def item(i, j):
                act.wait_ge(raw_loaded[j % RAW], i * (16 * BODY // RAW) + 16 * (j // RAW + 1))
                for n in range(UNITS):
                    wait(act, p1_done, per_item(i, j, UNITS, n + 1 - UNITS))
                    act.activation(a_hi[:, n], raw[:, j % RAW, n * UT:(n + 1) * UT, :], ACT.Copy)\
                       .then_inc(a_hi_ready, 1)
                if j % NG == 1 and j > NG:
                    slab_relu(slab_of(i, j), per_item(i, j - 1, 1, -NG + 2))
                if j == 0:
                    for n in range(RG // HC):
                        head(n)
                if j >= NG:
                    act.wait_ge(p2_done, per_item(i, j, 1, -NG + 1))
                for c in range(SC):
                    act.wait_ge(t_done, per_item(i, j, SC, c + 1))
                    act.activation(at_hi[:, (j % TRING) * SC + c, :], t_ps[:, c, :], ACT.Copy,
                                   accum_out=degp[:, (j // NG) % (BODY // NG), c, j % NG:j % NG + 1])\
                       .then_inc(at_hi_ready, 1)
                if j < NG - 1:
                    for n in range((j + 1) * RG // HC, (j + 2) * RG // HC):
                        head(n)
                if j % NG == NG - 1:
                    act.wait_ge(p1_done, per_item(i, j, UNITS, UNITS))
                    wait(act, msg_turned, slab_of(i, j))
                    act.activation(msgT[:, :], p1_ps[:, 0:SLAB], ACT.Copy).then_inc(msgT_copied, 1)

            def slab_relu(s, p2_before):
                act.wait_ge(norm_ready, s + NG)
                act.wait_ge(h2_ready, s)
                act.wait_ge(p2_done, p2_before)
                relu(u[:, 1], u[:, 0], h2_hi, norm)

            first_sweep(act, item)
            slab_relu(NS, ITEMS - NG + 2)

            act.wait_ge(p1_done, ITEMS * UNITS)
            def x1_hi(e):
                act.wait_ge(z_ready, e + 1)
                z = n1T[:, e * GROUP:(e + 1) * GROUP]
                act.activation(z, z, ACT.Silu).then_inc(act_step, 1)
                act.wait_ge(act_step, e + 1)
                act.activation(f_hi[:, e * GT:(e + 1) * GT], z.rearrange("p (t d) -> p t d", d=P), ACT.Copy)\
                   .then_inc(silu_done, 1)

            def hi3(g, j):
                if j in WHOLE3:
                    return
                act.wait_ge(t3_done, g * W3 + (j + 1))
                if not (isinstance(g, int) and g * W3 + j < RING3):
                    act.wait_ge(m3_done, g * W3 + (j - RING3 + 1))
                act.activation(at3_hi[:, j % RING3], turned[j % TURNED3][:, :, :], ACT.Copy)\
                   .then_inc(at3_hi_ready, 1)

            for e in range(4):
                x1_hi(e)
            for j in range(EARLY3):
                hi3(0, j)
            for e in range(4, 8):
                x1_hi(e)

            def group(g, parity, first):
                for j in range(EARLY3 if first else 0, W3):
                    hi3(g, j)
                    if j == 2 and not first:
                        copy_n2(g - 1, 1 - parity)
                    if j == 8 and not first:
                        silu3(g - 1, 1 - parity)
                    if j == 12 and not first:
                        store(g - 1, 1 - parity)

            def store(g, parity):
                act.wait_ge(y_ready, g + 1)
                act.dma_start(out_tiles[:, bass.ds(g * GT, GT), :],
                              tail[:, 1 + parity].rearrange("p (t d) -> p t d", d=P)).then_inc(y_out[parity], 16)

            def copy_n2(g, parity):
                act.wait_ge(m3_done, (g + 1) * W3)
                act.wait_ge(p2_done, 63 + 3)
                act.wait_ge(xw_done, g + 8)
                act.activation(tail[:, 0], p2_ps[:, parity, :], ACT.Copy).then_inc(n2_copied, 1)

            def silu3(g, parity):
                act.wait_ge(z_ready, g + 9)
                z = tail[:, 1 + parity]
                act.activation(z, z, ACT.Silu).then_inc(silu_done, 1)

            second_sweep(act, group)
            copy_n2(N3G - 1, 1)
            silu3(N3G - 1, 1)
            store(N3G - 1, 1)
            for stores in y_out:
                act.wait_ge(stores, 16 * (N3G // 2 + 1))

        SLAB_STEPS = 7
        HEAD_STEPS = NG

        @block.vector
        def _(dve):
            def chained(base):
                count = [0]

                def step(ins, between=lambda: None):
                    count[0] += 1
                    ins.then_inc(dve_step, 1)
                    between()
                    dve.wait_ge(dve_step, base + count[0])
                return step, count

            def statistics(step, src, dst, n):
                for t in range(n):
                    ins = dve.bn_stats(stats[:, t, :], src[:, t])
                step(ins)
                for t in range(n):
                    ins = dve.bn_aggr(dst[:, t, :], stats[:, t, :])
                ins.then_inc(mv_ready, 1)

            head_step, head_count = chained(0)

            def head_statistics(b):
                dve.wait_ge(x_loaded[b], 16)
                wait(dve, mv_ready, b)
                tiles = slice(b * RG, (b + 1) * RG)
                statistics(head_step, x[:, tiles], mv0[:, tiles], RG)

            def head_split(n):
                dve.wait_ge(u_ready, (n + 1) * UT // HC)
                tiles = slice(n * UT, (n + 1) * UT)
                dve.tensor_copy(f_hi[:, tiles], h_rows[:, tiles]).then_inc(h_hi_ready, 1)

            def slab_norm(i, j, work):
                s = slab_of(i, j)
                turn = (j // NG - 1) % (BODY // NG)
                chain, count = chained((s - 1) * SLAB_STEPS + HEAD_STEPS)

                def step(ins, n=None):
                    chain(ins, (lambda: work(n)) if n is not None else lambda: None)

                dve.wait_ge(at_hi_ready, per_item(i, j, SC))
                dve.wait_ge(u_ready, s - 1 + NT // HC)
                total, inv, clamped, finite, inv_deg = (deg[:, n, :] for n in range(5))
                step(dve.tensor_reduce(total, degp[:, turn], AX.X, ALU.add), 0)
                step(dve.reciprocal(inv, total), 1)
                step(dve.tensor_scalar(clamped, inv, -FLT_MAX, FLT_MAX, ALU.max, ALU.min), 2)
                step(dve.tensor_tensor(finite, inv, clamped, ALU.is_equal), 3)
                step(dve.tensor_tensor(inv_deg, clamped, finite, ALU.mult), 4)
                dve.wait_ge(msg_turned, s)
                for c in range(SC):
                    row = x[:, bass.ds((s - 1) * SC + c, 1), :]
                    ins = dve.scalar_tensor_tensor(
                        out=u[:, 1, c:c + 1, :], in0=m_ps[:, c * P:(c + 1) * P].rearrange("p (a d) -> p a d", a=1),
                        scalar=inv_deg[:, c:c + 1], in1=row, op0=ALU.mult, op1=ALU.add)
                step(ins)
                for c in range(SC):
                    ins = dve.bn_stats(stats[:, c, :], u[:, 1, c])
                step(ins)
                dve.tensor_scalar(x[:, bass.ds((s - 1) * SC, SC), :], u[:, 1], 1.0, None, ALU.mult)
                for c in range(SC):
                    ins = dve.bn_aggr(mv[:, c, :], stats[:, c, :])
                ins.then_inc(mv_ready, 1)
                assert count[0] == SLAB_STEPS

            def sum_n1(j, run, src=None):
                dve.wait_ge(p2_done, run + 1)
                g = (j - 6) % NG
                rows = n1T[:, g * QC:(g + 1) * QC].rearrange("p (m b c) -> p b m c", b=P // SB, c=SB)
                new = p2_ps[:, :, :].rearrange("p h n -> p (h n)") if src is None else src
                new = new.rearrange("p (b m c) -> p b m c", b=P // SB, c=SB)
                dve.tensor_tensor(rows, new, rows, ALU.add)\
                   .then_inc(n1_summed, 1)

            def item(i, j):
                if j == NG - 1:
                    dve.memset(p2_ps[:, :, :], 0.0).then_inc(p2_done, 1)
                if j == 0:
                    head_statistics(0)
                if j < NG - 1:
                    head_statistics(j + 1)
                def work(n):
                    if n < UNITS and (j % NG, n) not in POOL_UNITS:
                        a_lo_unit(dve, i, j, n, a_lo_dve)
                    if n == UNITS and j == 0:
                        for unit in range(UNITS):
                            head_split(unit)
                    if n == UNITS and j >= NG:
                        sum_n1(j, per_item(i, j, 1, -NG))
                    if n > UNITS:
                        c = n - UNITS - 1
                        slot = (j % TRING) * SC + c
                        dve.wait_ge(at_hi_ready, per_item(i, j, SC, c + 1))
                        dve.tensor_tensor(at_lo[:, slot, :], t_ps[:, c, :], at_hi[:, slot, :].bitcast(f32),
                                          ALU.subtract).then_inc(at_lo_ready, 1)

                if j % NG == 0 and j > 0:
                    slab_norm(i, j, work)
                else:
                    for n in range(UNITS + 1 + SC):
                        work(n)
                if j < NG - 1:
                    for n in range(UNITS):
                        head_split((j + 1) * UNITS + n)
                if j == NG - 1:
                    dve.wait_ge(n1_zeroed, NG)

            first_sweep(dve, item)
            slab_norm(0, ITEMS, lambda n: None)
            dve.wait_ge(y_out[1], 16)
            sum_n1(ITEMS, ITEMS - NG)
            sum_n1(ITEMS + 1, ITEMS - NG + 1)

            def add_bias(src, dst, done):
                four = "p (t d) -> p t d"
                dve.tensor_tensor(dst.rearrange(four, d=P), src.rearrange(four, d=P),
                                  bias[:, :].rearrange("p (a d) -> p a d", a=1).to_broadcast([P, GT, P]),
                                  ALU.add).then_inc(done, 1)

            def turn3(g, j):
                if j % WQ == 0:
                    dve.wait_ge(raw3_loaded[j // WQ], (g + 1) * 16 * (P // SB))
                if isinstance(g, int) and g == 0 and j == 2:
                    dve.wait_ge(p2_done, 63 + 3)
                turned_free(dve, g, j)
                m = (j % WQ) * UC
                src = raw3[j // WQ][:, :, m * SB:(m + UC) * SB].rearrange("p t (m c) -> p m t c", c=SB)
                dst = turned[j % TURNED3][:, :, :].rearrange("p m (t r) -> p m t r", r=SB)
                dve.transpose(dst, src).then_inc(t3_done, 1)

            def lo3_dve(g, j):
                if j not in WHOLE3:
                    lo3_part(dve, g, j, slice(POOL_ROWS, GROUP), at3_lo_dve)

            for g in range(NG):
                sum_n1(ITEMS + 2 + g, ITEMS - NG + 2 + g, [t_ps[:, 0, :], None][g % 2])
                if g == NG - 2:
                    for j in range(EARLY3):
                        turn3(0, j)
                    for j in range(EARLY3 - 1):
                        lo3_dve(0, j)
                for e in (2 * g, 2 * g + 1):
                    dve.wait_ge(xw_done, e + 1)
                    add_bias([p1_ps, m_ps][e % 2][:, :], n1T[:, e * GROUP:(e + 1) * GROUP], z_ready)

            def group(g, parity, first):
                for j in range(EARLY3 if first else 0, W3):
                    turn3(g, j)
                    if j > 0:
                        lo3_dve(g, j - 1)
                    elif not first:
                        lo3_dve(g - 1, W3 - 1)
                    if j == 8 and not first:
                        bias3(g - 1, 1 - parity)
                    if j == 12 and not first:
                        residual(g - 1, 1 - parity)

            def bias3(g, parity):
                dve.wait_ge(xw_done, g + 9)
                dve.wait_ge(y_out[parity], g * 8 + (16 - 8 * parity))
                add_bias(p1_ps[:, :], tail[:, 1 + parity], z_ready)

            def residual(g, parity):
                dve.wait_ge(silu_done, g + 9)
                y = tail[:, 1 + parity].rearrange("p (t d) -> p t d", d=P)
                dve.tensor_tensor(y, y, x[:, bass.ds(g * GT, GT), :], ALU.add).then_inc(y_ready, 1)

            second_sweep(dve, group)
            lo3_dve(N3G - 1, W3 - 1)
            bias3(N3G - 1, 1)
            residual(N3G - 1, 1)

        @block.gpsimd
        def _(pool):
            for n, value in enumerate((EPS, -1.0, -0.5)):
                pool.memset(consts[:, n:n + 1], value)
            pool.memset(ident[:, :], 0.0).then_inc(pool_const, 1)
            pool.wait_ge(pool_const, 1)
            pool.affine_select(out=ident[:, :], in_=ident[:, :], compare_op=ALU.not_equal, fill=1.0,
                               base=0, pattern=[[-1, P]], channel_multiplier=1).then_inc(consts_ready, 1)
            pool.memset(h2_hi[:, :, :].bitcast(f32), 0.0)
            pool.memset(h2_lo[:, :, :].bitcast(f32), 0.0).then_inc(at_lo_ready, SC)

            last = (TRING - 1) * SC
            pool.memset(at_hi[:, last:last + SC, :].bitcast(f32), 0.0)
            pool.memset(at_lo[:, last:last + SC, :].bitcast(f32), 0.0).then_inc(h2_ready, 1)

            def zeros(j):
                pool.wait_ge(h_ready, (j + 1) * UNITS)
                pool.memset(n1T[:, j * QC:(j + 1) * QC], 0.0).then_inc(n1_zeroed, 1)

            def scale_shift(stat, dst, n, before):
                eps, minus, power = (consts[:, m:m + 1].to_broadcast([P, n]) for m in range(3))
                pool.tensor_tensor(dst[:, 0], stat[:, :, 1], eps, ALU.add)
                pool.tensor_tensor(dst[:, 1], stat[:, :, 0], minus, ALU.mult).then_inc(pool_step, 1)
                pool.wait_ge(pool_step, before + 1)
                pool.tensor_tensor(dst[:, 2], dst[:, 0], power, ALU.pow).then_inc(pool_step, 1)
                pool.wait_ge(pool_step, before + 2)
                pool.tensor_tensor(dst[:, 3], dst[:, 1], dst[:, 2], ALU.mult).then_inc(norm_ready, 1)

            def head(b):
                pool.wait_ge(mv_ready, b + 1)
                tiles = slice(b * RG, (b + 1) * RG)
                scale_shift(mv0[:, tiles], norm0[:, :, tiles], RG, 2 * b)

            def head_lo(n):
                pool.wait_ge(h_hi_ready, n + 1)
                tiles = slice(n * UT, (n + 1) * UT)
                pool.tensor_tensor(f_lo[:, tiles], h_rows[:, tiles], f_hi[:, tiles].bitcast(f32),
                                   ALU.subtract).then_inc(h_ready, 1)

            def split_h2(i, j):
                s = slab_of(i, j)
                pool.wait_ge(mv_ready, s + NG)
                scale_shift(mv, norm, HC, (NG + s - 1) * 2)
                pool.wait_ge(u_ready, s + NT // HC)
                pool.tensor_tensor(h2_lo[:, :, :], u[:, 0], h2_hi[:, :, :].bitcast(f32), ALU.subtract)\
                    .then_inc(h2_ready, 1)

            def item(i, j):
                if j == 0:
                    head(0)
                if j < NG - 1:
                    head(j + 1)
                for n in range(UNITS):
                    if (j % NG, n) in POOL_UNITS:
                        a_lo_unit(pool, i, j, n, a_lo_pool)
                    if j == 0:
                        head_lo(n)
                if j < NG - 1:
                    for n in range(UNITS):
                        head_lo((j + 1) * UNITS + n)
                if j < NG:
                    zeros(j)
                if j % NG == 0 and j > 0:
                    split_h2(i, j)

            first_sweep(pool, item)
            split_h2(0, ITEMS)
            def x1_lo(e):
                pool.wait_ge(silu_done, e + 1)
                at = slice(e * GT, (e + 1) * GT)
                pool.tensor_tensor(f_lo[:, at], n1T[:, e * GROUP:(e + 1) * GROUP].rearrange("p (t d) -> p t d", d=P),
                                   f_hi[:, at].bitcast(f32), ALU.subtract).then_inc(x1_ready, 1)

            def lo3_pool(g, j):
                if j not in WHOLE3:
                    lo3_part(pool, g, j, slice(0, POOL_ROWS), at3_lo_pool)

            for e in range(4):
                x1_lo(e)
            for j in range(EARLY3):
                lo3_pool(0, j)
            for e in range(4, 8):
                x1_lo(e)

            def group(g, parity, first):
                for j in range(EARLY3 if first else 0, W3):
                    lo3_pool(g, j)

            second_sweep(pool, group)


_INS = ["x", "adj", "L1_gnn_W", "L1_gnn_b"]


def kernel(**inputs):
    import numpy as _np
    import concourse.bacc as _bacc
    from concourse import mybir as _mybir
    from concourse.bass_utils import run_bass_kernel_spmd as _run

    nc = _bacc.Bacc("TRN2", target_bir_lowering=False, num_devices=1)
    arrays, args = {}, []
    for name in _INS:
        a = _np.ascontiguousarray(inputs[name])
        arrays[f"in_{name}_dram"] = a
        args.append(nc.dram_tensor(f"in_{name}_dram", a.shape, _mybir.dt.from_np(a.dtype), kind="ExternalInput").ap())
    args.append(nc.dram_tensor("out_dram", (N, P), _mybir.dt.float32, kind="ExternalOutput").ap())
    build(nc, *args)
    r = _run(nc, [arrays], core_ids=[0])
    return r.results[0]["out_dram"]
```
